# Optimizing a Trainium2 kernel written in Bass

```python
import numpy as np
import jax
import jax.numpy as jnp

def _softmax(x, axis=-1):
    return jax.nn.softmax(x, axis=axis)
def _gelu(x):
    return jax.nn.gelu(x, approximate=True)
def _silu(x):
    return jax.nn.silu(x)
def _sigmoid(x):
    return jax.nn.sigmoid(x)
def _layernorm(x, axis=-1, eps=1e-5):
    m = jnp.mean(x, axis=axis, keepdims=True)
    v = jnp.var(x, axis=axis, keepdims=True)
    return (x - m) / jnp.sqrt(v + eps)
def _scatter_add(tgt, idx, src, axis=0):
    return tgt.at[idx].add(src)
def _segment_sum(src, seg, n):
    return jax.ops.segment_sum(src, seg, n)

kernel_name = 'mk_conv_preact_d1_conv_nchw768_4b3d23'

def setup_inputs(seed: int = 0):
    np.random.seed(seed)
    _w = jnp.asarray
    def _rec_inputs():
        import jax
        import jax.numpy as jnp
        _gk = jax.random.key(seed)
        x = -4.65e-05 + 0.9999 * jax.random.normal(jax.random.fold_in(_gk, 1), (16, 768, 64, 64), jnp.float32)
        return x
    x = _rec_inputs()
    def _L0_conv_setup():
        import jax, jax.numpy as jnp
        from jax import lax
        import numpy as np
        H = W = 64
        SCALE = 64.0
        STRIDE = 16
        CHAN_PER_POS = 16
        KSIZE = 3
        SIGMA = 0.5
        BATCH = 16

        def _init_offset_grid():
            offs = []
            n = 3
            for ih in range(-n, n + 1):
                for iw in range(-n, n + 1):
                    if ih == 0 and iw == 0:
                        continue
                    offs.append([iw * STRIDE / SCALE, ih * STRIDE / SCALE])
            return np.array(offs, dtype=np.float32)

        def _displace(x, offset):
            B, C, h, w = x.shape
            F_off = offset.shape[0]
            bind = C // F_off
            off_px = offset * SCALE
            off_int = lax.stop_gradient(jnp.round(off_px))
            sub = off_px - off_int
            dx = jnp.repeat(off_int[:, 0].astype(jnp.int32), bind)
            dy = jnp.repeat(off_int[:, 1].astype(jnp.int32), bind)
            iy = jnp.arange(h)[None, :] - dy[:, None]
            ix = jnp.arange(w)[None, :] - dx[:, None]
            vy = (iy >= 0) & (iy < h)
            vx = (ix >= 0) & (ix < w)
            iyc = jnp.clip(iy, 0, h - 1)
            ixc = jnp.clip(ix, 0, w - 1)
            ch = jnp.arange(C)
            shifted = x[:, ch[:, None, None], iyc[:, :, None], ixc[:, None, :]]
            mask = (vy[:, :, None] & vx[:, None, :]).astype(x.dtype)
            shifted = shifted * mask[None]
            r = jnp.arange(KSIZE, dtype=x.dtype) - KSIZE // 2
            fx = r[None, :]
            fy = r[:, None]
            kx = fx[None] + sub[:, 0][:, None, None]
            ky = fy[None] + sub[:, 1][:, None, None]
            kern = jnp.exp(-(kx * kx + ky * ky) / (2.0 * SIGMA * SIGMA))
            kern = kern / kern.sum(axis=(1, 2), keepdims=True)
            kern_c = jnp.repeat(kern, bind, axis=0)
            out = lax.conv_general_dilated(shifted, kern_c[:, None, :, :], window_strides=(1, 1), padding='SAME', feature_group_count=C, dimension_numbers=('NCHW', 'OIHW', 'NCHW'))
            return out
        key = jax.random.key(seed)
        k1, k2 = jax.random.split(key)
        C = 48 * CHAN_PER_POS
        x = jax.random.normal(k1, (BATCH, C, H, W), dtype=jnp.float32)
        offset = jnp.asarray(_init_offset_grid()) + 0.01 * jax.random.normal(k2, (48, 2), dtype=jnp.float32)
        return {'x': x, 'offset': offset}
    _L0_conv_all = _L0_conv_setup()
    _L0_conv_in = {k: v for k, v in _L0_conv_all.items() if k in ('offset', )}
    del _L0_conv_all

    return {
        "x": x,
        "L0_conv_offset": _L0_conv_in["offset"],
    }

def reference(x, L0_conv_offset):
    import jax
    import jax.numpy as jnp
    def _L0_conv_ref(x, offset):
        import jax, jax.numpy as jnp
        from jax import lax
        import numpy as np
        H = W = 64
        SCALE = 64.0
        STRIDE = 16
        CHAN_PER_POS = 16
        KSIZE = 3
        SIGMA = 0.5
        BATCH = 16

        def _init_offset_grid():
            offs = []
            n = 3
            for ih in range(-n, n + 1):
                for iw in range(-n, n + 1):
                    if ih == 0 and iw == 0:
                        continue
                    offs.append([iw * STRIDE / SCALE, ih * STRIDE / SCALE])
            return np.array(offs, dtype=np.float32)

        def _displace(x, offset):
            B, C, h, w = x.shape
            F_off = offset.shape[0]
            bind = C // F_off
            off_px = offset * SCALE
            off_int = lax.stop_gradient(jnp.round(off_px))
            sub = off_px - off_int
            dx = jnp.repeat(off_int[:, 0].astype(jnp.int32), bind)
            dy = jnp.repeat(off_int[:, 1].astype(jnp.int32), bind)
            iy = jnp.arange(h)[None, :] - dy[:, None]
            ix = jnp.arange(w)[None, :] - dx[:, None]
            vy = (iy >= 0) & (iy < h)
            vx = (ix >= 0) & (ix < w)
            iyc = jnp.clip(iy, 0, h - 1)
            ixc = jnp.clip(ix, 0, w - 1)
            ch = jnp.arange(C)
            shifted = x[:, ch[:, None, None], iyc[:, :, None], ixc[:, None, :]]
            mask = (vy[:, :, None] & vx[:, None, :]).astype(x.dtype)
            shifted = shifted * mask[None]
            r = jnp.arange(KSIZE, dtype=x.dtype) - KSIZE // 2
            fx = r[None, :]
            fy = r[:, None]
            kx = fx[None] + sub[:, 0][:, None, None]
            ky = fy[None] + sub[:, 1][:, None, None]
            kern = jnp.exp(-(kx * kx + ky * ky) / (2.0 * SIGMA * SIGMA))
            kern = kern / kern.sum(axis=(1, 2), keepdims=True)
            kern_c = jnp.repeat(kern, bind, axis=0)
            out = lax.conv_general_dilated(shifted, kern_c[:, None, :, :], window_strides=(1, 1), padding='SAME', feature_group_count=C, dimension_numbers=('NCHW', 'OIHW', 'NCHW'))
            return out
        return _displace(x, offset)

    def _gn(v, G=32, eps=1e-5):
        B_, C_, H_, W_ = v.shape
        g = v.reshape(B_, G, C_ // G, H_, W_)
        m = jnp.mean(g, axis=(2, 3, 4), keepdims=True)
        s = jnp.var(g, axis=(2, 3, 4), keepdims=True)
        return ((g - m) / jnp.sqrt(s + eps)).reshape(v.shape)

    def _ln_c(v, eps=1e-6):
        m = jnp.mean(v, axis=1, keepdims=True)
        s = jnp.var(v, axis=1, keepdims=True)
        return (v - m) / jnp.sqrt(s + eps)

    def _ln_t(v, eps=1e-5):
        m = jnp.mean(v, axis=-1, keepdims=True)
        s = jnp.var(v, axis=-1, keepdims=True)
        return (v - m) / jnp.sqrt(s + eps)

    def _to_tokens(v):
        B_, C_, H_, W_ = v.shape
        return v.reshape(B_, C_, H_ * W_).transpose(0, 2, 1)
    def _from_tokens(t, like):
        B_, C_, H_, W_ = like.shape
        return t.transpose(0, 2, 1).reshape(B_, C_, H_, W_)

    x = x + _L0_conv_ref(_gn(x), L0_conv_offset)
    return x


_drawn_inputs = setup_inputs


def setup_inputs(seed=0):
    import zlib

    import numpy as np

    out = dict(_drawn_inputs(seed))
    spreads = {}
    factors = {}
    for name, (base, spread) in spreads.items():
        noise = np.random.default_rng([zlib.crc32(name.encode()), seed]).standard_normal(out[name].shape)
        drawn = base * np.exp(spread * noise) if base else spread * noise
        out[name] = jnp.asarray(drawn.astype(out[name].dtype))
    for name, factor in factors.items():
        out[name] = (out[name] * factor).astype(out[name].dtype)
    return out
```

```python
import concourse.bass as bass
from concourse import mybir
from contextlib import ExitStack


def build(nc, x, offset, out):
    f32 = mybir.dt.float32
    i32 = mybir.dt.int32
    bf16 = mybir.dt.bfloat16
    ALU = mybir.AluOpType
    ACT = mybir.ActivationFunctionType

    P = 128
    BATCH, CHANNELS, H, W = x.shape
    PIX = H * W
    POSITIONS = offset.shape[0]
    TILE_CH = P // BATCH
    TILES = CHANNELS // TILE_CH
    TILES_PER_POSITION = CHANNELS // POSITIONS // TILE_CH
    GROUPS = 32
    GT = TILES // GROUPS
    GROUP_N = GT * TILE_CH * PIX
    SLOT_GROUPS = 3
    SLOTS = SLOT_GROUPS * GT
    ROUNDS = GROUPS // SLOT_GROUPS
    SCALE = 64.0
    EPS = 1e-5
    BANK = 512
    CHUNKS = PIX // BANK

    SIDES = [H, 52, 36, 20]
    LEAST = [0] + [H + 1 - s for s in SIDES[1:]]
    MOST = [a - 1 for a in LEAST[1:]] + [H]
    PAD = max(m + s - H for m, s in zip(MOST, SIDES))
    LEFT = PAD + 1
    PITCH = W + LEFT
    FRAME_ROWS = PAD + H + PAD + 2

    x_tiles = x.rearrange("b (j c) h w -> j b c (h w)", c=TILE_CH)
    out_tiles = out.rearrange("b (j c) h w -> j b c (h w)", c=TILE_CH)

    ctx = ExitStack()
    with ctx:
        def sb(name, shape, dt=f32):
            return ctx.enter_context(nc.sbuf_tensor(name, shape, dt))

        def pb(name, shape, dt=f32):
            return ctx.enter_context(nc.psum_tensor(name, shape, dt))

        def sem(name):
            return ctx.enter_context(nc.semaphore(name))

        xs = sb("xs", [P, SLOTS * PIX + W])
        frame = sb("frame", [P, FRAME_ROWS * PITCH])
        smooth = sb("smooth", [P, PIX])
        same_image = sb("same_image", [P, P])
        unused = sb("unused", [P, PIX], bf16)
        zeros = sb("zeros", [P, H])
        eps = sb("eps", [P, 1])
        neg_mean = sb("neg_mean", [P, SLOT_GROUPS])
        squares = sb("squares", [P, SLOTS])
        std = sb("std", [P, 1])
        var = sb("var", [P, 1])
        rstd0 = sb("rstd0", [P, 1])
        fix = sb("fix", [P, 2])
        rstd = sb("rstd", [P, 1])
        col_w = sb("col_w", [P, 3])

        side_w = sb("side_w", [P, POSITIONS, 2])
        base_w = sb("base_w", [P, POSITIONS, 3])
        table = sb("table", [P, POSITIONS, 4], i32)
        setup = smooth[:, 0:10 * 2 * POSITIONS].rearrange("p (n f a) -> p n f a", n=10, a=2)
        off = setup[:, 0]
        whole = setup[:, 1]
        rest = setup[:, 2]
        tmp = setup[:, 3]
        norm = setup[:, 4]
        kind = setup[:, 5]
        start = setup[:, 6]
        e = setup[:, 7:10]
        KIND, FROM, TO, EDGE = range(4)

        sum_ps = [pb(f"sum_ps{i}", [P, BANK]) for i in range(SLOT_GROUPS)]
        var_ps = pb("var_ps", [P, BANK])

        frame_v = frame[:, :].rearrange("p (r c) -> p r c", c=PITCH)
        frame_image = frame_v[:, PAD:PAD + H, LEFT:LEFT + W]

        loaded = [sem(f"loaded{s}") for s in range(SLOTS)]
        stored = [sem(f"stored{s}") for s in range(SLOTS)]
        offset_loaded = sem("offset_loaded")
        selector_step = sem("selector_step")
        selector_ready = sem("selector_ready")
        zeros_ready = sem("zeros_ready")
        exp_args_ready = sem("exp_args_ready")
        exps_ready = sem("exps_ready")
        setup_step = sem("setup_step")
        table_ready = sem("table_ready")
        sums_ready = sem("sums_ready")
        mean_ready = sem("mean_ready")
        squares_ready = sem("squares_ready")
        var_ready = sem("var_ready")
        std_ready = sem("std_ready")
        frame_copied = sem("frame_copied")
        frame_ready = sem("frame_ready")
        half_smooth = sem("half_smooth")
        smooth_ready = sem("smooth_ready")
        rstd_step = sem("rstd_step")
        col_w_ready = sem("col_w_ready")
        centre_added = sem("centre_added")
        above_added = sem("above_added")
        tile_done = sem("tile_done")

        block = ctx.enter_context(nc.Block())

        def slot_px(s, a=0, b=PIX):
            return xs[:, s * PIX + a:s * PIX + b]

        @block.sync
        def _(sp):
            sp.dma_start(off[:, :, :], offset.partition_broadcast(P)).then_inc(offset_loaded, 16)

            def load(tile, s):
                sp.dma_start(slot_px(s), x_tiles[tile]).then_inc(loaded[s], 16)

            def store(tile, s):
                sp.wait_ge(tile_done, tile + 2)
                sp.dma_start(out_tiles[tile], slot_px(s)).then_inc(stored[s], 16)

            def round_of(k, refills):
                for s in range(SLOTS):
                    store(k * SLOTS + s, s)
                    if 1 <= s <= refills:
                        sp.wait_ge(stored[s - 1], 16 * (k + 1))
                        load((k + 1) * SLOTS + s - 1, s - 1)
                if refills == SLOTS:
                    sp.wait_ge(stored[SLOTS - 1], 16 * (k + 1))
                    load((k + 1) * SLOTS + SLOTS - 1, SLOTS - 1)

            for s in range(SLOTS):
                load(s, s)
            with sp.Fori(0, ROUNDS - 1) as k:
                round_of(k, SLOTS)
            rest_tiles = TILES - ROUNDS * SLOTS
            round_of(ROUNDS - 1, rest_tiles)
            for s in range(rest_tiles):
                store(ROUNDS * SLOTS + s, s)
            for s in range(SLOTS):
                sp.wait_ge(stored[s], 16 * (ROUNDS + (s < rest_tiles)))

        @block.gpsimd
        def _(pool):
            nc.gpsimd.memset(zeros[:, :], 0.0)
            nc.gpsimd.memset(eps[:, :], EPS)
            nc.gpsimd.memset(frame[:, :], 0.0).then_inc(zeros_ready, 1)
            nc.gpsimd.memset(same_image[:, :], 1.0).then_inc(selector_step, 1)
            v = same_image[:, :].rearrange("p (b c) -> p b c", c=TILE_CH)
            pool.wait_ge(selector_step, 1)
            nc.gpsimd.affine_select(out=v, in_=v, compare_op=ALU.is_ge, fill=0.0, base=0,
                                    pattern=[[-TILE_CH, BATCH], [0, TILE_CH]],
                                    channel_multiplier=1).then_inc(selector_step, 1)
            pool.wait_ge(selector_step, 2)
            nc.gpsimd.affine_select(out=v, in_=v, compare_op=ALU.is_ge, fill=0.0, base=TILE_CH - 1,
                                    pattern=[[TILE_CH, BATCH], [0, TILE_CH]],
                                    channel_multiplier=-1).then_inc(selector_ready, 1)

        @block.tensor
        def _(pe):
            pe.wait_ge(selector_ready, 1)

            def sum_tile(b, i, k):
                s = b * GT + i
                pe.wait_ge(loaded[s], 16 * (k + 1))
                for c in range(CHUNKS):
                    last = nc.tensor.matmul(sum_ps[b][:, :], same_image[:, :],
                                            slot_px(s, c * BANK, (c + 1) * BANK),
                                            start=(i == 0 and c == 0), stop=(i == GT - 1 and c == CHUNKS - 1))
                if i == GT - 1:
                    last.then_inc(sums_ready, 1)

            def sum_squares(group, b):
                pe.wait_ge(squares_ready, GT * (group + 1))
                for i in range(GT):
                    s = b * GT + i
                    last = nc.tensor.matmul(var_ps[:, 0:1], same_image[:, :], squares[:, s:s + 1],
                                            start=(i == 0), stop=(i == GT - 1))
                last.then_inc(var_ready, 1)

            def group_of(k, b, first=False):
                sum_tile(b, 0, k)
                if not first:
                    sum_squares(k * SLOT_GROUPS + b - 1, (b - 1) % SLOT_GROUPS)
                for i in range(1, GT):
                    sum_tile(b, i, k)

            for b in range(SLOT_GROUPS):
                group_of(0, b, first=(b == 0))
            with pe.Fori(1, ROUNDS) as k:
                for b in range(SLOT_GROUPS):
                    group_of(k, b)
            left = GROUPS - ROUNDS * SLOT_GROUPS
            for b in range(left):
                group_of(ROUNDS, b)
            sum_squares(GROUPS - 1, left - 1)

        @block.scalar
        def _(act):
            act.wait_ge(exp_args_ready, 1)
            nc.scalar.activation(e[:, :, :, :], e[:, :, :, :], ACT.Exp, scale=-2.0).then_inc(exps_ready, 1)
            act.wait_ge(zeros_ready, 1)
            act.wait_ge(table_ready, 1)

            def mean(group, b):
                act.wait_ge(sums_ready, group + 1)
                nc.scalar.activation(sum_ps[b][:, :], sum_ps[b][:, :], ACT.Copy, scale=-1.0 / GROUP_N,
                                     accum_out=neg_mean[:, b:b + 1]).then_inc(mean_ready, 1)

            def square(group, b, i, first=False):
                s = b * GT + i
                if not first:
                    act.wait_ge(squares_ready, group * GT + i)
                nc.scalar.activation(unused[:, :], slot_px(s), ACT.Square, bias=neg_mean[:, b:b + 1],
                                     accum_out=squares[:, s:s + 1]).then_inc(squares_ready, 1)

            def fill_frame(group, b, i, first=False):
                tile = group * GT + i
                if not first:
                    act.wait_ge(smooth_ready, tile)
                nc.scalar.activation(frame_image, slot_px(b * GT + i).rearrange("p (r c) -> p r c", c=W),
                                     ACT.Identity, bias=neg_mean[:, b:b + 1]).then_inc(frame_copied, 1)
                position = tile // TILES_PER_POSITION
                edge = act.value_load(table[0:1, bass.ds(position, 1), EDGE:EDGE + 1],
                                      min_val=LEFT - 1, max_val=LEFT + W - 1)
                act.wait_ge(frame_copied, tile + 1)
                nc.scalar.activation(frame_v[:, PAD:PAD + H, bass.ds(edge, 1)],
                                     zeros[:, :].rearrange("p (r c) -> p r c", c=1),
                                     ACT.Copy).then_inc(frame_ready, 1)

            def deviation(group):
                act.wait_ge(var_ready, group + 1)
                nc.scalar.activation(std[:, :], var_ps[:, 0:1], ACT.Sqrt, bias=eps[:, :],
                                     scale=1.0 / GROUP_N).then_inc(std_ready, 1)

            def window(group, b, first=False, last=False):
                nb = (b + 1) % SLOT_GROUPS
                fill_frame(group, b, 0, first)
                deviation(group)
                fill_frame(group, b, 1)
                if not last:
                    mean(group + 1, nb)
                    act.wait_ge(mean_ready, group + 2)
                    square(group + 1, nb, 0)
                    square(group + 1, nb, 1)
                fill_frame(group, b, 2)
                if not last:
                    square(group + 1, nb, 2)

            mean(0, 0)
            act.wait_ge(mean_ready, 1)
            for i in range(GT):
                square(0, 0, i, first=(i == 0))
            for b in range(SLOT_GROUPS):
                window(b, b, first=(b == 0))
            with act.Fori(1, ROUNDS) as k:
                for b in range(SLOT_GROUPS):
                    window(k * SLOT_GROUPS + b, b)
            for g in range(ROUNDS * SLOT_GROUPS, GROUPS):
                window(g, g % SLOT_GROUPS, last=(g == GROUPS - 1))

        @block.vector
        def _(dve):
            steps = [0]

            def chained(ins):
                steps[0] += 1
                ins.then_inc(setup_step, 1)
                dve.wait_ge(setup_step, steps[0])

            V = nc.vector
            dve.wait_ge(offset_loaded, 16)
            FAR, ROUNDER = 1024.0, 1.5 * 2.0 ** 23
            chained(V.tensor_scalar(off[:, :, :], off[:, :, :], SCALE, FAR, ALU.mult, ALU.min))
            chained(V.tensor_scalar(off[:, :, :], off[:, :, :], -FAR, None, ALU.max))
            chained(V.tensor_scalar(whole[:, :, :], off[:, :, :], ROUNDER, None, ALU.add))
            chained(V.tensor_scalar(whole[:, :, :], whole[:, :, :], ROUNDER, None, ALU.subtract))
            chained(V.tensor_tensor(rest[:, :, :], off[:, :, :], whole[:, :, :], ALU.subtract))
            for k in range(3):
                chained(V.tensor_scalar(tmp[:, :, :], rest[:, :, :], float(k - 1), None, ALU.add))
                last = V.tensor_tensor(e[:, k], tmp[:, :, :], tmp[:, :, :], ALU.mult)
                if k < 2:
                    chained(last)
            last.then_inc(exp_args_ready, 1)

            chained(V.tensor_scalar(whole[:, :, :], whole[:, :, :], float(H), -float(H), ALU.min, ALU.max))
            size_d, below, shrink = tmp, norm, start
            chained(V.scalar_tensor_tensor(size_d[:, :, :], whole[:, :, :], -1.0, whole[:, :, :],
                                           ALU.mult, ALU.max))
            for n, least in enumerate(LEAST[1:]):
                step = float(SIDES[n] - SIDES[n + 1])
                to = kind if n == 0 else below
                chained(V.tensor_scalar(to[:, :, :], size_d[:, :, :], float(least), None, ALU.is_ge))
                if n == 0:
                    chained(V.tensor_scalar(shrink[:, :, :], to[:, :, :], step, None, ALU.mult))
                else:
                    chained(V.tensor_tensor(kind[:, :, :], kind[:, :, :], to[:, :, :], ALU.add))
                    chained(V.scalar_tensor_tensor(shrink[:, :, :], to[:, :, :], step, shrink[:, :, :],
                                                   ALU.mult, ALU.add))
            positive, window, edge = below, size_d, off
            chained(V.tensor_scalar(positive[:, :, :], whole[:, :, :], 0.0, None, ALU.is_gt))
            chained(V.tensor_tensor(start[:, :, :], shrink[:, :, :], positive[:, :, :], ALU.mult))
            chained(V.tensor_tensor(window[:, :, :], start[:, :, :], whole[:, :, :], ALU.subtract))
            chained(V.scalar_tensor_tensor(edge[:, :, :], positive[:, :, :], float(W + 1), whole[:, :, :],
                                           ALU.mult, ALU.subtract))
            chained(V.tensor_scalar(table[:, :, EDGE], edge[:, :, 0], float(LEFT - 1), None, ALU.add))
            chained(V.scalar_tensor_tensor(table[:, :, KIND], kind[:, :, 1], float(len(SIDES)),
                                           kind[:, :, 0], ALU.mult, ALU.add))
            chained(V.scalar_tensor_tensor(table[:, :, TO], start[:, :, 1], float(W), start[:, :, 0],
                                           ALU.mult, ALU.add))
            chained(V.scalar_tensor_tensor(edge[:, :, 1], window[:, :, 1], float(PITCH), window[:, :, 0],
                                           ALU.mult, ALU.add))
            V.tensor_scalar(table[:, :, FROM], edge[:, :, 1], float(PAD * PITCH + LEFT), None,
                            ALU.add).then_inc(table_ready, 1)

            dve.wait_ge(exps_ready, 1)
            chained(V.tensor_tensor(norm[:, :, :], e[:, 0], e[:, 1], ALU.add))
            chained(V.tensor_tensor(norm[:, :, :], norm[:, :, :], e[:, 2], ALU.add))
            chained(V.reciprocal(norm[:, :, :], norm[:, :, :]))
            chained(V.reciprocal(tmp[:, :, 0], e[:, 1, :, 0]))
            chained(V.tensor_tensor(side_w[:, :, 0], e[:, 0, :, 0], tmp[:, :, 0], ALU.mult))
            chained(V.tensor_tensor(side_w[:, :, 1], e[:, 2, :, 0], tmp[:, :, 0], ALU.mult))
            chained(V.tensor_tensor(tmp[:, :, 0], e[:, 1, :, 0], norm[:, :, 0], ALU.mult))
            chained(V.tensor_tensor(tmp[:, :, 0], tmp[:, :, 0], norm[:, :, 1], ALU.mult))
            for k in range(3):
                last = V.tensor_tensor(base_w[:, :, k], e[:, k, :, 1], tmp[:, :, 0], ALU.mult)
            last.then_inc(tile_done, 1)

            def reciprocal_std(group):
                dve.wait_ge(std_ready, group + 1)
                V.reciprocal(rstd0[:, :], std[:, :]).then_inc(rstd_step, 1)
                V.tensor_scalar(var[:, :], var_ps[:, 0:1], 1.0 / GROUP_N, EPS, ALU.mult,
                                ALU.add).then_inc(rstd_step, 1)
                dve.wait_ge(rstd_step, 5 * group + 2)
                V.tensor_scalar(fix[:, 0:1], var[:, :], rstd0[:, :], rstd0[:, :], ALU.mult,
                                ALU.mult).then_inc(rstd_step, 1)
                dve.wait_ge(rstd_step, 5 * group + 3)
                V.tensor_scalar(fix[:, 1:2], fix[:, 0:1], -0.5, 1.5, ALU.mult, ALU.add).then_inc(rstd_step, 1)
                dve.wait_ge(rstd_step, 5 * group + 4)
                V.tensor_tensor(rstd[:, :], fix[:, 1:2], rstd0[:, :], ALU.mult).then_inc(rstd_step, 1)
                dve.wait_ge(rstd_step, 5 * group + 5)

            def smooth_tile(rows, cols, group, i, tile, position, src, dst):
                def frame_window(shift):
                    v = frame[:, bass.ds(src + shift, rows * PITCH)]
                    return v.rearrange("p (r c) -> p r c", c=PITCH)[:, :, 0:cols]

                def x_window(a, b):
                    v = xs[:, bass.ds(dst + a * W, (b - a) * W)]
                    return v.rearrange("p (r c) -> p r c", c=W)[:, :, 0:cols]

                dve.wait_ge(tile_done, tile + 1)
                dve.wait_ge(frame_ready, tile + 1)
                sm = smooth[:, 0:rows * cols].rearrange("p (r c) -> p r c", c=cols)
                V.scalar_tensor_tensor(sm, frame_window(-1), side_w[:, bass.ds(position, 1), 0], frame_window(0),
                                       ALU.mult, ALU.add).then_inc(half_smooth, 1)
                dve.wait_ge(half_smooth, tile + 1)
                V.scalar_tensor_tensor(sm, frame_window(1), side_w[:, bass.ds(position, 1), 1], sm,
                                       ALU.mult, ALU.add).then_inc(smooth_ready, 1)
                if i == 0:
                    reciprocal_std(group)
                V.tensor_scalar(col_w[:, :], base_w[:, bass.ds(position, 1), :].rearrange("p a k -> p (a k)"),
                                rstd[:, :], None, ALU.mult).then_inc(col_w_ready, 1)
                dve.wait_ge(smooth_ready, tile + 1)
                dve.wait_ge(col_w_ready, tile + 1)
                V.scalar_tensor_tensor(x_window(0, rows), sm, col_w[:, 1:2], x_window(0, rows),
                                       ALU.mult, ALU.add).then_inc(centre_added, 1)
                dve.wait_ge(centre_added, tile + 1)
                V.scalar_tensor_tensor(x_window(1, rows), sm[:, 0:rows - 1], col_w[:, 0:1], x_window(1, rows),
                                       ALU.mult, ALU.add).then_inc(above_added, 1)
                dve.wait_ge(above_added, tile + 1)
                V.scalar_tensor_tensor(x_window(0, rows - 1), sm[:, 1:rows], col_w[:, 2:3], x_window(0, rows - 1),
                                       ALU.mult, ALU.add).then_inc(tile_done, 1)

            def choose(kind_of, low, high, emit):
                if high - low == 1:
                    emit(low)
                    return
                middle = (low + high) // 2
                with dve.If(kind_of < middle):
                    choose(kind_of, low, middle, emit)
                with dve.Else():
                    choose(kind_of, middle, high, emit)

            with dve.Fori(0, GROUPS) as g:
                base = (g % SLOT_GROUPS) * (GT * PIX)
                for i in range(GT):
                    tile = g * GT + i
                    position = tile // TILES_PER_POSITION
                    def entry(n, top):
                        return dve.value_load(table[0:1, bass.ds(position, 1), n:n + 1], min_val=0, max_val=top)
                    kind_of = entry(KIND, len(SIDES) ** 2 - 1)
                    src = entry(FROM, FRAME_ROWS * PITCH)
                    dst = entry(TO, (H - SIDES[-1]) * (W + 1))

                    def emit(code):
                        ky, kx = divmod(code, len(SIDES))
                        rows, cols = SIDES[ky], SIDES[kx]
                        most = (PAD + MOST[ky]) * PITCH + LEFT + MOST[kx]
                        smooth_tile(rows, cols, g, i, tile, position,
                                    src.with_bounds(min_val=1, max_val=most),
                                    (base + i * PIX + dst).with_bounds(min_val=0, max_val=(SLOTS - 1) * PIX + (H - rows) * W + W - cols))

                    choose(kind_of, 0, len(SIDES) ** 2, emit)


def kernel(x, L0_conv_offset):
    import numpy as np
    import concourse.bacc as bacc
    from concourse.bass_utils import run_bass_kernel_spmd

    nc = bacc.Bacc("TRN2", target_bir_lowering=False, num_devices=1)
    arrays = {"x_dram": np.ascontiguousarray(x), "offset_dram": np.ascontiguousarray(L0_conv_offset)}
    aps = [nc.dram_tensor(name, a.shape, mybir.dt.from_np(a.dtype), kind="ExternalInput").ap()
           for name, a in arrays.items()]
    out = nc.dram_tensor("out_dram", x.shape, mybir.dt.float32, kind="ExternalOutput").ap()
    build(nc, *aps, out)
    r = run_bass_kernel_spmd(nc, [arrays], core_ids=[0])
    return r.results[0]["out_dram"]
```

```python
import concourse.bass as bass
from concourse import mybir
from contextlib import ExitStack


def build(nc, x, offset, out):
    f32 = mybir.dt.float32
    i32 = mybir.dt.int32
    bf16 = mybir.dt.bfloat16
    ALU = mybir.AluOpType
    ACT = mybir.ActivationFunctionType

    P = 128
    BATCH, CHANNELS, H, W = x.shape
    PIX = H * W
    POSITIONS = offset.shape[0]
    TILE_CH = P // BATCH
    TILES = CHANNELS // TILE_CH
    TILES_PER_POSITION = CHANNELS // POSITIONS // TILE_CH
    GROUPS = 32
    GT = TILES // GROUPS
    GROUP_N = GT * TILE_CH * PIX
    SLOT_GROUPS = 3
    SLOTS = SLOT_GROUPS * GT
    ROUNDS = GROUPS // SLOT_GROUPS
    SCALE = 64.0
    EPS = 1e-5
    BANK = 512
    CHUNKS = PIX // BANK

    SIDES = [H, 52, 36, 20]
    LEAST = [0] + [H + 1 - s for s in SIDES[1:]]
    MOST = [a - 1 for a in LEAST[1:]] + [H]
    PAD = max(m + s - H for m, s in zip(MOST, SIDES))
    LEFT = PAD + 1
    PITCH = W + LEFT
    FRAME_ROWS = PAD + H + PAD + 2

    STRIDE, FIRST = 19, 9

    def group_at(turn):
        return (turn * STRIDE + FIRST) % GROUPS

    x_tiles = x.rearrange("b (j c) h w -> j b c (h w)", c=TILE_CH)
    out_tiles = out.rearrange("b (j c) h w -> j b c (h w)", c=TILE_CH)

    ctx = ExitStack()
    with ctx:
        def sb(name, shape, dt=f32):
            return ctx.enter_context(nc.sbuf_tensor(name, shape, dt))

        def pb(name, shape, dt=f32):
            return ctx.enter_context(nc.psum_tensor(name, shape, dt))

        def sem(name):
            return ctx.enter_context(nc.semaphore(name))

        xs = sb("xs", [P, SLOTS * PIX + W])
        frame = sb("frame", [P, FRAME_ROWS * PITCH])
        smooth = sb("smooth", [P, PIX])
        same_image = sb("same_image", [P, P])
        unused = sb("unused", [P, PIX], bf16)
        zeros = sb("zeros", [P, H])
        neg_mean = sb("neg_mean", [P, SLOT_GROUPS])
        neg_pivot = sb("neg_pivot", [P, SLOT_GROUPS])
        squares = sb("squares", [P, SLOTS])
        std = sb("std", [P, 1])
        mean_off = sb("mean_off", [P, 1])
        square_mean = sb("square_mean", [P, 1])
        neg_var = sb("neg_var", [P, 1])
        rstd0 = sb("rstd0", [P, 1])
        fix = sb("fix", [P, 2])
        rstd = sb("rstd", [P, 1])
        col_w = sb("col_w", [P, 3])

        side_w = sb("side_w", [P, POSITIONS, 2])
        base_w = sb("base_w", [P, POSITIONS, 3])
        windows = sb("windows", [P, POSITIONS], i32)
        edges = sb("edges", [P, POSITIONS], i32)
        setup = smooth[:, 0:10 * 2 * POSITIONS].rearrange("p (n f a) -> p n f a", n=10, a=2)
        off = setup[:, 0]
        whole = setup[:, 1]
        rest = setup[:, 2]
        tmp = setup[:, 3]
        norm = setup[:, 4]
        kind = setup[:, 5]
        start = setup[:, 6]
        e = setup[:, 7:10]
        parts = smooth[:, 20 * POSITIONS:23 * POSITIONS].bitcast(i32).rearrange("p (n f) -> p n f", n=3)
        KIND, TO, FROM = range(3)
        KIND_BITS = (len(SIDES) ** 2 - 1).bit_length()
        TO_BITS = ((H - SIDES[-1]) * (W + 1)).bit_length()

        sum_ps = [pb(f"sum_ps{i}", [P, BANK]) for i in range(SLOT_GROUPS)]
        pivot_ps = [pb(f"pivot_ps{i}", [P, BANK]) for i in range(SLOT_GROUPS)]
        var_ps = pb("var_ps", [P, BANK])

        frame_v = frame[:, :].rearrange("p (r c) -> p r c", c=PITCH)
        frame_image = frame_v[:, PAD:PAD + H, LEFT:LEFT + W]

        loaded = [sem(f"loaded{s}") for s in range(SLOTS)]
        stored = [sem(f"stored{s}") for s in range(SLOTS)]
        offset_loaded = sem("offset_loaded")
        selector_step = sem("selector_step")
        selector_ready = sem("selector_ready")
        zeros_ready = sem("zeros_ready")
        exp_args_ready = sem("exp_args_ready")
        exps_ready = sem("exps_ready")
        setup_step = sem("setup_step")
        table_ready = sem("table_ready")
        pivot_sum_ready = sem("pivot_sum_ready")
        pivot_ready = sem("pivot_ready")
        neg_var_ready = sem("neg_var_ready")
        sums_ready = sem("sums_ready")
        mean_ready = sem("mean_ready")
        squares_ready = sem("squares_ready")
        var_ready = sem("var_ready")
        std_ready = sem("std_ready")
        frame_copied = sem("frame_copied")
        frame_ready = sem("frame_ready")
        half_smooth = sem("half_smooth")
        smooth_ready = sem("smooth_ready")
        std_step = sem("std_step")
        col_w_ready = sem("col_w_ready")
        centre_added = sem("centre_added")
        above_added = sem("above_added")
        tile_done = sem("tile_done")

        block = ctx.enter_context(nc.Block())

        def slot_px(s, a=0, b=PIX):
            return xs[:, s * PIX + a:s * PIX + b]

        @block.sync
        def _(sp):
            sp.dma_start(off[:, :, :], offset.partition_broadcast(P)).then_inc(offset_loaded, 16)

            def source_tile(k, s):
                return group_at(k * SLOT_GROUPS + s // GT) * GT + s % GT

            def load(k, s):
                sp.dma_start(slot_px(s), x_tiles[source_tile(k, s)]).then_inc(loaded[s], 16)

            def store(k, s):
                sp.wait_ge(tile_done, k * SLOTS + s + 2)
                sp.dma_start(out_tiles[source_tile(k, s)], slot_px(s)).then_inc(stored[s], 16)

            def round_of(k, refills):
                for s in range(SLOTS):
                    store(k, s)
                    if 1 <= s <= refills:
                        sp.wait_ge(stored[s - 1], 16 * (k + 1))
                        load(k + 1, s - 1)
                if refills == SLOTS:
                    sp.wait_ge(stored[SLOTS - 1], 16 * (k + 1))
                    load(k + 1, SLOTS - 1)

            for s in range(SLOTS):
                load(0, s)
            with sp.Fori(0, ROUNDS - 1) as k:
                round_of(k, SLOTS)
            rest_tiles = TILES - ROUNDS * SLOTS
            round_of(ROUNDS - 1, rest_tiles)
            for s in range(rest_tiles):
                store(ROUNDS, s)
            for s in range(SLOTS):
                sp.wait_ge(stored[s], 16 * (ROUNDS + (s < rest_tiles)))

        @block.gpsimd
        def _(pool):
            nc.gpsimd.memset(zeros[:, :], 0.0)
            nc.gpsimd.memset(frame[:, :], 0.0).then_inc(zeros_ready, 1)
            nc.gpsimd.memset(same_image[:, :], 1.0).then_inc(selector_step, 1)
            v = same_image[:, :].rearrange("p (b c) -> p b c", c=TILE_CH)
            pool.wait_ge(selector_step, 1)
            nc.gpsimd.affine_select(out=v, in_=v, compare_op=ALU.is_ge, fill=0.0, base=0,
                                    pattern=[[-TILE_CH, BATCH], [0, TILE_CH]],
                                    channel_multiplier=1).then_inc(selector_step, 1)
            pool.wait_ge(selector_step, 2)
            nc.gpsimd.affine_select(out=v, in_=v, compare_op=ALU.is_ge, fill=0.0, base=TILE_CH - 1,
                                    pattern=[[TILE_CH, BATCH], [0, TILE_CH]],
                                    channel_multiplier=-1).then_inc(selector_ready, 1)

        @block.tensor
        def _(pe):
            pe.wait_ge(selector_ready, 1)
            SQUARES_AT = 1

            def sum_tile(b, i, k):
                s = b * GT + i
                pe.wait_ge(loaded[s], 16 * (k + 1))
                if i == 0:
                    nc.tensor.matmul(pivot_ps[b][:, :], same_image[:, :], slot_px(s, 0, BANK),
                                     start=True, stop=True).then_inc(pivot_sum_ready, 1)
                for c in range(CHUNKS):
                    last = nc.tensor.matmul(sum_ps[b][:, :], same_image[:, :],
                                            slot_px(s, c * BANK, (c + 1) * BANK),
                                            start=(i == 0 and c == 0), stop=(i == GT - 1 and c == CHUNKS - 1))
                if i == GT - 1:
                    last.then_inc(sums_ready, 1)

            def sum_squares(turn, b):
                pe.wait_ge(squares_ready, GT * (turn + 1))
                for i in range(GT):
                    s = b * GT + i
                    last = nc.tensor.matmul(var_ps[:, 0:1], same_image[:, :], squares[:, s:s + 1],
                                            start=(i == 0), stop=(i == GT - 1))
                last.then_inc(var_ready, 1)

            def group_of(k, b, first=False):
                for i in range(GT):
                    if i == SQUARES_AT and not first:
                        sum_squares(k * SLOT_GROUPS + b - 1, (b - 1) % SLOT_GROUPS)
                    sum_tile(b, i, k)

            for b in range(SLOT_GROUPS):
                group_of(0, b, first=(b == 0))
            with pe.Fori(1, ROUNDS) as k:
                for b in range(SLOT_GROUPS):
                    group_of(k, b)
            left = GROUPS - ROUNDS * SLOT_GROUPS
            for b in range(left):
                group_of(ROUNDS, b)
            sum_squares(GROUPS - 1, left - 1)

        @block.scalar
        def _(act):
            act.wait_ge(exp_args_ready, 1)
            nc.scalar.activation(e[:, :, :, :], e[:, :, :, :], ACT.Exp, scale=-2.0).then_inc(exps_ready, 1)
            act.wait_ge(zeros_ready, 1)
            act.wait_ge(table_ready, 1)

            def pivot(turn, b):
                act.wait_ge(pivot_sum_ready, turn + 1)
                nc.scalar.activation(pivot_ps[b][:, :], pivot_ps[b][:, :], ACT.Copy,
                                     scale=-1.0 / (TILE_CH * BANK),
                                     accum_out=neg_pivot[:, b:b + 1]).then_inc(pivot_ready, 1)

            def mean(turn, b):
                act.wait_ge(sums_ready, turn + 1)
                nc.scalar.activation(sum_ps[b][:, :], sum_ps[b][:, :], ACT.Copy, scale=-1.0 / GROUP_N,
                                     accum_out=neg_mean[:, b:b + 1]).then_inc(mean_ready, 1)

            def square(k, b, i, first=False):
                k, b = k + b // SLOT_GROUPS, b % SLOT_GROUPS
                turn, s = k * SLOT_GROUPS + b, b * GT + i
                if i:
                    act.wait_ge(loaded[s], 16 * (k + 1))
                else:
                    act.wait_ge(pivot_ready, turn + 1)
                if not first:
                    act.wait_ge(squares_ready, turn * GT + i)
                nc.scalar.activation(unused[:, :], slot_px(s), ACT.Square, bias=neg_pivot[:, b:b + 1],
                                     accum_out=squares[:, s:s + 1]).then_inc(squares_ready, 1)

            def fill_frame(turn, b, i, first=False):
                tile = turn * GT + i
                if not first:
                    act.wait_ge(smooth_ready, tile)
                nc.scalar.activation(frame_image, slot_px(b * GT + i).rearrange("p (r c) -> p r c", c=W),
                                     ACT.Identity, bias=neg_mean[:, b:b + 1]).then_inc(frame_copied, 1)
                position = (group_at(turn) * GT + i) // TILES_PER_POSITION
                edge = act.value_load(edges[0:1, bass.ds(position, 1)],
                                      min_val=LEFT - 1, max_val=LEFT + W - 1)
                act.wait_ge(frame_copied, tile + 1)
                nc.scalar.activation(frame_v[:, PAD:PAD + H, bass.ds(edge, 1)],
                                     zeros[:, :].rearrange("p (r c) -> p r c", c=1),
                                     ACT.Copy).then_inc(frame_ready, 1)

            def deviation(turn):
                act.wait_ge(neg_var_ready, turn + 1)
                nc.scalar.activation(std[:, :], neg_var[:, :], ACT.Sqrt, scale=-1.0).then_inc(std_ready, 1)

            def turn_of(k, b, ahead=GROUPS):
                turn = k * SLOT_GROUPS + b
                act.wait_ge(mean_ready, turn + 1)
                fill_frame(turn, b, 0, first=(ahead == GROUPS - 1))
                if ahead >= 1:
                    square(k, b + 1, 1)
                deviation(turn)
                fill_frame(turn, b, 1)
                if ahead >= 1:
                    square(k, b + 1, 2)
                fill_frame(turn, b, 2)
                if ahead >= 1:
                    mean(turn + 1, (b + 1) % SLOT_GROUPS)
                if ahead >= 2:
                    pivot(turn + 2, (b + 2) % SLOT_GROUPS)
                    square(k, b + 2, 0)

            pivot(0, 0)
            for i in range(GT):
                square(0, 0, i, first=(i == 0))
            mean(0, 0)
            pivot(1, 1)
            square(0, 1, 0)
            for b in range(SLOT_GROUPS):
                turn_of(0, b, ahead=GROUPS - 1 - b)
            with act.Fori(1, ROUNDS) as k:
                for b in range(SLOT_GROUPS):
                    turn_of(k, b)
            left = GROUPS - ROUNDS * SLOT_GROUPS
            for b in range(left):
                turn_of(ROUNDS, b, ahead=left - 1 - b)

        @block.vector
        def _(dve):
            steps = [0]

            def chained(ins):
                steps[0] += 1
                ins.then_inc(setup_step, 1)
                dve.wait_ge(setup_step, steps[0])

            V = nc.vector
            dve.wait_ge(offset_loaded, 16)
            FAR, ROUNDER = 1024.0, 1.5 * 2.0 ** 23
            chained(V.tensor_scalar(off[:, :, :], off[:, :, :], SCALE, FAR, ALU.mult, ALU.min))
            chained(V.tensor_scalar(off[:, :, :], off[:, :, :], -FAR, None, ALU.max))
            chained(V.tensor_scalar(whole[:, :, :], off[:, :, :], ROUNDER, None, ALU.add))
            chained(V.tensor_scalar(whole[:, :, :], whole[:, :, :], ROUNDER, None, ALU.subtract))
            chained(V.tensor_tensor(rest[:, :, :], off[:, :, :], whole[:, :, :], ALU.subtract))
            for k in range(3):
                chained(V.tensor_scalar(tmp[:, :, :], rest[:, :, :], float(k - 1), None, ALU.add))
                last = V.tensor_tensor(e[:, k], tmp[:, :, :], tmp[:, :, :], ALU.mult)
                if k < 2:
                    chained(last)
            last.then_inc(exp_args_ready, 1)

            chained(V.tensor_scalar(whole[:, :, :], whole[:, :, :], float(H), -float(H), ALU.min, ALU.max))
            size_d, below, shrink = tmp, norm, start
            chained(V.scalar_tensor_tensor(size_d[:, :, :], whole[:, :, :], -1.0, whole[:, :, :],
                                           ALU.mult, ALU.max))
            for n, least in enumerate(LEAST[1:]):
                step = float(SIDES[n] - SIDES[n + 1])
                to = kind if n == 0 else below
                chained(V.tensor_scalar(to[:, :, :], size_d[:, :, :], float(least), None, ALU.is_ge))
                if n == 0:
                    chained(V.tensor_scalar(shrink[:, :, :], to[:, :, :], step, None, ALU.mult))
                else:
                    chained(V.tensor_tensor(kind[:, :, :], kind[:, :, :], to[:, :, :], ALU.add))
                    chained(V.scalar_tensor_tensor(shrink[:, :, :], to[:, :, :], step, shrink[:, :, :],
                                                   ALU.mult, ALU.add))
            positive, window, edge = below, size_d, off
            chained(V.tensor_scalar(positive[:, :, :], whole[:, :, :], 0.0, None, ALU.is_gt))
            chained(V.tensor_tensor(start[:, :, :], shrink[:, :, :], positive[:, :, :], ALU.mult))
            chained(V.tensor_tensor(window[:, :, :], start[:, :, :], whole[:, :, :], ALU.subtract))
            chained(V.scalar_tensor_tensor(edge[:, :, :], positive[:, :, :], float(W + 1), whole[:, :, :],
                                           ALU.mult, ALU.subtract))
            chained(V.tensor_scalar(edges[:, :], edge[:, :, 0], float(LEFT - 1), None, ALU.add))
            chained(V.scalar_tensor_tensor(parts[:, KIND], kind[:, :, 1], float(len(SIDES)),
                                           kind[:, :, 0], ALU.mult, ALU.add))
            chained(V.scalar_tensor_tensor(parts[:, TO], start[:, :, 1], float(W), start[:, :, 0],
                                           ALU.mult, ALU.add))
            chained(V.scalar_tensor_tensor(edge[:, :, 1], window[:, :, 1], float(PITCH), window[:, :, 0],
                                           ALU.mult, ALU.add))
            chained(V.tensor_scalar(parts[:, FROM], edge[:, :, 1], float(PAD * PITCH + LEFT), None, ALU.add))
            chained(V.tensor_scalar(parts[:, TO], parts[:, TO], KIND_BITS, None, ALU.logical_shift_left))
            chained(V.tensor_scalar(parts[:, FROM], parts[:, FROM], KIND_BITS + TO_BITS, None,
                                    ALU.logical_shift_left))
            chained(V.tensor_tensor(windows[:, :], parts[:, KIND], parts[:, TO], ALU.bitwise_or))
            V.tensor_tensor(windows[:, :], windows[:, :], parts[:, FROM], ALU.bitwise_or).then_inc(table_ready, 1)

            dve.wait_ge(exps_ready, 1)
            chained(V.tensor_tensor(norm[:, :, :], e[:, 0], e[:, 1], ALU.add))
            chained(V.tensor_tensor(norm[:, :, :], norm[:, :, :], e[:, 2], ALU.add))
            chained(V.reciprocal(norm[:, :, :], norm[:, :, :]))
            chained(V.reciprocal(tmp[:, :, 0], e[:, 1, :, 0]))
            chained(V.tensor_tensor(side_w[:, :, 0], e[:, 0, :, 0], tmp[:, :, 0], ALU.mult))
            chained(V.tensor_tensor(side_w[:, :, 1], e[:, 2, :, 0], tmp[:, :, 0], ALU.mult))
            chained(V.tensor_tensor(tmp[:, :, 0], e[:, 1, :, 0], norm[:, :, 0], ALU.mult))
            chained(V.tensor_tensor(tmp[:, :, 0], tmp[:, :, 0], norm[:, :, 1], ALU.mult))
            for k in range(3):
                last = V.tensor_tensor(base_w[:, :, k], e[:, k, :, 1], tmp[:, :, 0], ALU.mult)
            last.then_inc(tile_done, 1)

            STD_STEPS = 6

            def variance(turn, b):
                dve.wait_ge(var_ready, turn + 1)
                V.tensor_scalar(square_mean[:, :], var_ps[:, 0:1], 1.0 / GROUP_N, EPS, ALU.mult,
                                ALU.add).then_inc(std_step, 1)
                dve.wait_ge(mean_ready, turn + 1)
                V.tensor_tensor(mean_off[:, :], neg_pivot[:, bass.ds(b, 1)], neg_mean[:, bass.ds(b, 1)],
                                ALU.subtract).then_inc(std_step, 1)
                dve.wait_ge(std_step, STD_STEPS * turn + 2)
                V.scalar_tensor_tensor(neg_var[:, :], mean_off[:, :], mean_off[:, :], square_mean[:, :],
                                       ALU.mult, ALU.subtract).then_inc(neg_var_ready, 1)

            def reciprocal_std(turn):
                dve.wait_ge(std_ready, turn + 1)
                V.reciprocal(rstd0[:, :], std[:, :]).then_inc(std_step, 1)
                dve.wait_ge(std_step, STD_STEPS * turn + 3)
                V.tensor_scalar(fix[:, 0:1], neg_var[:, :], rstd0[:, :], rstd0[:, :], ALU.mult,
                                ALU.mult).then_inc(std_step, 1)
                dve.wait_ge(std_step, STD_STEPS * turn + 4)
                V.tensor_scalar(fix[:, 1:2], fix[:, 0:1], 0.5, 1.5, ALU.mult, ALU.add).then_inc(std_step, 1)
                dve.wait_ge(std_step, STD_STEPS * turn + 5)
                V.tensor_tensor(rstd[:, :], fix[:, 1:2], rstd0[:, :], ALU.mult).then_inc(std_step, 1)
                dve.wait_ge(std_step, STD_STEPS * turn + 6)

            def smooth_tile(rows, cols, turn, i, tile, position, follows, src, dst):
                def frame_window(shift):
                    v = frame[:, bass.ds(src + shift, rows * PITCH)]
                    return v.rearrange("p (r c) -> p r c", c=PITCH)[:, :, 0:cols]

                def x_window(a, b):
                    v = xs[:, bass.ds(dst + a * W, (b - a) * W)]
                    return v.rearrange("p (r c) -> p r c", c=W)[:, :, 0:cols]

                dve.wait_ge(tile_done, tile + 1)
                dve.wait_ge(frame_ready, tile + 1)
                sm = smooth[:, 0:rows * cols].rearrange("p (r c) -> p r c", c=cols)
                V.scalar_tensor_tensor(sm, frame_window(-1), side_w[:, bass.ds(position, 1), 0], frame_window(0),
                                       ALU.mult, ALU.add).then_inc(half_smooth, 1)
                load_window(follows)
                dve.wait_ge(half_smooth, tile + 1)
                V.scalar_tensor_tensor(sm, frame_window(1), side_w[:, bass.ds(position, 1), 1], sm,
                                       ALU.mult, ALU.add).then_inc(smooth_ready, 1)
                if i == 0:
                    reciprocal_std(turn)
                V.tensor_scalar(col_w[:, :], base_w[:, bass.ds(position, 1), :].rearrange("p a k -> p (a k)"),
                                rstd[:, :], None, ALU.mult).then_inc(col_w_ready, 1)
                dve.wait_ge(smooth_ready, tile + 1)
                dve.wait_ge(col_w_ready, tile + 1)
                V.scalar_tensor_tensor(x_window(0, rows), sm, col_w[:, 1:2], x_window(0, rows),
                                       ALU.mult, ALU.add).then_inc(centre_added, 1)
                dve.wait_ge(centre_added, tile + 1)
                V.scalar_tensor_tensor(x_window(1, rows), sm[:, 0:rows - 1], col_w[:, 0:1], x_window(1, rows),
                                       ALU.mult, ALU.add).then_inc(above_added, 1)
                dve.wait_ge(above_added, tile + 1)
                V.scalar_tensor_tensor(x_window(0, rows - 1), sm[:, 1:rows], col_w[:, 2:3], x_window(0, rows - 1),
                                       ALU.mult, ALU.add).then_inc(tile_done, 1)

            def choose(kind_of, low, high, emit):
                if high - low == 1:
                    emit(low)
                    return
                middle = (low + high) // 2
                with dve.If(kind_of < middle):
                    choose(kind_of, low, middle, emit)
                with dve.Else():
                    choose(kind_of, middle, high, emit)

            next_window = dve.alloc_register("next_window")

            def load_window(position):
                dve.reg_load(next_window, windows[0:1, bass.ds(position, 1)])

            def position_of(turn, i):
                return (group_at(turn) * GT + i) // TILES_PER_POSITION

            dve.wait_ge(table_ready, 1)
            load_window(position_of(0, 0))
            with dve.Fori(0, GROUPS) as turn:
                variance(turn, turn % SLOT_GROUPS)
                base = (turn % SLOT_GROUPS) * (GT * PIX)
                for i in range(GT):
                    tile = turn * GT + i
                    position = position_of(turn, i)
                    follows = position_of(turn, i + 1) if i + 1 < GT else position_of(turn + 1, 0)
                    entry = dve.snap(next_window, min_val=0, max_val=(FRAME_ROWS * PITCH << KIND_BITS + TO_BITS) - 1)
                    kind_of = dve.snap(entry & (1 << KIND_BITS) - 1)
                    dst = (entry >> KIND_BITS) & (1 << TO_BITS) - 1
                    src = entry >> KIND_BITS + TO_BITS

                    def emit(code):
                        ky, kx = divmod(code, len(SIDES))
                        rows, cols = SIDES[ky], SIDES[kx]
                        most = (PAD + MOST[ky]) * PITCH + LEFT + MOST[kx]
                        smooth_tile(rows, cols, turn, i, tile, position, follows,
                                    src.with_bounds(min_val=1, max_val=most),
                                    (base + i * PIX + dst).with_bounds(min_val=0, max_val=(SLOTS - 1) * PIX + (H - rows) * W + W - cols))

                    choose(kind_of, 0, len(SIDES) ** 2, emit)


def kernel(x, L0_conv_offset):
    import numpy as np
    import concourse.bacc as bacc
    from concourse.bass_utils import run_bass_kernel_spmd

    nc = bacc.Bacc("TRN2", target_bir_lowering=False, num_devices=1)
    arrays = {"x_dram": np.ascontiguousarray(x), "offset_dram": np.ascontiguousarray(L0_conv_offset)}
    aps = [nc.dram_tensor(name, a.shape, mybir.dt.from_np(a.dtype), kind="ExternalInput").ap()
           for name, a in arrays.items()]
    out = nc.dram_tensor("out_dram", x.shape, mybir.dt.float32, kind="ExternalOutput").ap()
    build(nc, *aps, out)
    r = run_bass_kernel_spmd(nc, [arrays], core_ids=[0])
    return r.results[0]["out_dram"]
```

```python
import concourse.bass as bass
from concourse import mybir
from contextlib import ExitStack


def build(nc, x, offset, out):
    f32 = mybir.dt.float32
    i32 = mybir.dt.int32
    bf16 = mybir.dt.bfloat16
    ALU = mybir.AluOpType
    ACT = mybir.ActivationFunctionType

    P = 128
    BATCH, CHANNELS, H, W = x.shape
    PIX = H * W
    POSITIONS = offset.shape[0]
    TILE_CH = P // BATCH
    TILES = CHANNELS // TILE_CH
    TILES_PER_POSITION = CHANNELS // POSITIONS // TILE_CH
    GROUPS = 32
    GT = TILES // GROUPS
    GROUP_N = GT * TILE_CH * PIX
    SLOT_GROUPS = 3
    SLOTS = SLOT_GROUPS * GT
    ROUNDS = GROUPS // SLOT_GROUPS
    SCALE = 64.0
    EPS = 1e-5
    BANK = 512
    CHUNKS = PIX // BANK

    SIDES = [H, 50, 34, 18]
    LEAST = [0] + [H + 1 - s for s in SIDES[1:]]
    MOST = [a - 1 for a in LEAST[1:]] + [H]
    PAD = max(m + s - H for m, s in zip(MOST, SIDES))
    LEFT = PAD + 1
    PITCH = W + LEFT
    FRAME_ROWS = PAD + H + PAD + 2

    STRIDE, FIRST = 11, 8

    def group_at(turn):
        return (turn * STRIDE + FIRST) % GROUPS

    x_tiles = x.rearrange("b (j c) h w -> j b c (h w)", c=TILE_CH)
    out_tiles = out.rearrange("b (j c) h w -> j b c (h w)", c=TILE_CH)

    ctx = ExitStack()
    with ctx:
        def sb(name, shape, dt=f32):
            return ctx.enter_context(nc.sbuf_tensor(name, shape, dt))

        def pb(name, shape, dt=f32):
            return ctx.enter_context(nc.psum_tensor(name, shape, dt))

        def sem(name):
            return ctx.enter_context(nc.semaphore(name))

        xs = sb("xs", [P, SLOTS * PIX + W])
        frame = sb("frame", [P, FRAME_ROWS * PITCH])
        smooth = sb("smooth", [P, PIX])
        same_image = sb("same_image", [P, P])
        unused = sb("unused", [P, PIX], bf16)
        zeros = sb("zeros", [P, H])
        neg_mean = sb("neg_mean", [P, SLOT_GROUPS])
        neg_pivot = sb("neg_pivot", [P, SLOT_GROUPS])
        squares = sb("squares", [P, SLOTS])
        std = sb("std", [P, 1])
        mean_off = sb("mean_off", [P, 1])
        square_mean = sb("square_mean", [P, 1])
        neg_var = sb("neg_var", [P, 1])
        rstd0 = sb("rstd0", [P, 1])
        fix = sb("fix", [P, 2])
        rstd = sb("rstd", [P, 1])
        col_w = sb("col_w", [P, 3])

        side_w = sb("side_w", [P, POSITIONS, 2])
        base_w = sb("base_w", [P, POSITIONS, 3])
        windows = sb("windows", [P, POSITIONS], i32)
        fills = sb("fills", [P, POSITIONS], i32)
        setup = smooth[:, 0:10 * 2 * POSITIONS].rearrange("p (n f a) -> p n f a", n=10, a=2)
        off = setup[:, 0]
        whole = setup[:, 1]
        rest = setup[:, 2]
        tmp = setup[:, 3]
        norm = setup[:, 4]
        kind = setup[:, 5]
        shrink = setup[:, 6]
        e = setup[:, 7:10]
        parts = smooth[:, 20 * POSITIONS:23 * POSITIONS].bitcast(i32).rearrange("p (n f) -> p n f", n=3)
        KIND, TO, FROM = range(3)
        KIND_BITS = (len(SIDES) ** 2 - 1).bit_length()
        TO_BITS = ((H - SIDES[-1]) * (W + 1)).bit_length()
        EDGE_BITS = (PITCH - 1).bit_length()
        ROW_BITS = (H - SIDES[-1]).bit_length()

        sum_ps = [pb(f"sum_ps{i}", [P, BANK]) for i in range(SLOT_GROUPS)]
        pivot_ps = [pb(f"pivot_ps{i}", [P, BANK]) for i in range(SLOT_GROUPS)]
        var_ps = pb("var_ps", [P, BANK])

        xs_v = xs[:, :].rearrange("p (r c) -> p r c", c=W)
        frame_v = frame[:, :].rearrange("p (r c) -> p r c", c=PITCH)

        loaded = [sem(f"loaded{s}") for s in range(SLOTS)]
        stored = [sem(f"stored{s}") for s in range(SLOTS)]
        offset_loaded = sem("offset_loaded")
        selector_step = sem("selector_step")
        selector_ready = sem("selector_ready")
        zeros_ready = sem("zeros_ready")
        exp_args_ready = sem("exp_args_ready")
        exps_ready = sem("exps_ready")
        setup_step = sem("setup_step")
        table_ready = sem("table_ready")
        pivot_sum_ready = sem("pivot_sum_ready")
        pivot_ready = sem("pivot_ready")
        neg_var_ready = sem("neg_var_ready")
        sums_ready = sem("sums_ready")
        mean_ready = sem("mean_ready")
        squares_ready = sem("squares_ready")
        var_ready = sem("var_ready")
        std_ready = sem("std_ready")
        frame_copied = sem("frame_copied")
        frame_ready = sem("frame_ready")
        half_smooth = sem("half_smooth")
        smooth_ready = sem("smooth_ready")
        std_step = sem("std_step")
        col_w_ready = sem("col_w_ready")
        centre_added = sem("centre_added")
        above_added = sem("above_added")
        tile_done = sem("tile_done")

        block = ctx.enter_context(nc.Block())

        def slot_px(s, a=0, b=PIX):
            return xs[:, s * PIX + a:s * PIX + b]

        def choose(engine, value, low, high, emit):
            if high - low == 1:
                emit(low)
                return
            middle = (low + high) // 2
            with engine.If(value < middle):
                choose(engine, value, low, middle, emit)
            with engine.Else():
                choose(engine, value, middle, high, emit)

        @block.sync
        def _(sp):
            sp.dma_start(off[:, :, :], offset.partition_broadcast(P)).then_inc(offset_loaded, 16)

            def source_tile(k, s):
                return group_at(k * SLOT_GROUPS + s // GT) * GT + s % GT

            def load(k, s):
                sp.dma_start(slot_px(s), x_tiles[source_tile(k, s)]).then_inc(loaded[s], 16)

            def store(k, s):
                sp.wait_ge(tile_done, k * SLOTS + s + 2)
                sp.dma_start(out_tiles[source_tile(k, s)], slot_px(s)).then_inc(stored[s], 16)

            def round_of(k, refills):
                for s in range(SLOTS):
                    store(k, s)
                    if 1 <= s <= refills:
                        sp.wait_ge(stored[s - 1], 16 * (k + 1))
                        load(k + 1, s - 1)
                if refills == SLOTS:
                    sp.wait_ge(stored[SLOTS - 1], 16 * (k + 1))
                    load(k + 1, SLOTS - 1)

            for s in range(SLOTS):
                load(0, s)
            with sp.Fori(0, ROUNDS - 1) as k:
                round_of(k, SLOTS)
            rest_tiles = TILES - ROUNDS * SLOTS
            round_of(ROUNDS - 1, rest_tiles)
            for s in range(rest_tiles):
                store(ROUNDS, s)
            for s in range(SLOTS):
                sp.wait_ge(stored[s], 16 * (ROUNDS + (s < rest_tiles)))

        @block.gpsimd
        def _(pool):
            nc.gpsimd.memset(zeros[:, :], 0.0)
            nc.gpsimd.memset(frame[:, :], 0.0).then_inc(zeros_ready, 1)
            nc.gpsimd.memset(same_image[:, :], 1.0).then_inc(selector_step, 1)
            v = same_image[:, :].rearrange("p (b c) -> p b c", c=TILE_CH)
            pool.wait_ge(selector_step, 1)
            nc.gpsimd.affine_select(out=v, in_=v, compare_op=ALU.is_ge, fill=0.0, base=0,
                                    pattern=[[-TILE_CH, BATCH], [0, TILE_CH]],
                                    channel_multiplier=1).then_inc(selector_step, 1)
            pool.wait_ge(selector_step, 2)
            nc.gpsimd.affine_select(out=v, in_=v, compare_op=ALU.is_ge, fill=0.0, base=TILE_CH - 1,
                                    pattern=[[TILE_CH, BATCH], [0, TILE_CH]],
                                    channel_multiplier=-1).then_inc(selector_ready, 1)

        @block.tensor
        def _(pe):
            pe.wait_ge(selector_ready, 1)
            SQUARES_AT = 1

            def sum_tile(b, i, k):
                s = b * GT + i
                pe.wait_ge(loaded[s], 16 * (k + 1))
                if i == 0:
                    nc.tensor.matmul(pivot_ps[b][:, :], same_image[:, :], slot_px(s, 0, BANK),
                                     start=True, stop=True).then_inc(pivot_sum_ready, 1)
                for c in range(CHUNKS):
                    last = nc.tensor.matmul(sum_ps[b][:, :], same_image[:, :],
                                            slot_px(s, c * BANK, (c + 1) * BANK),
                                            start=(i == 0 and c == 0), stop=(i == GT - 1 and c == CHUNKS - 1))
                if i == GT - 1:
                    last.then_inc(sums_ready, 1)

            def sum_squares(turn, b):
                pe.wait_ge(squares_ready, GT * (turn + 1))
                for i in range(GT):
                    s = b * GT + i
                    last = nc.tensor.matmul(var_ps[:, 0:1], same_image[:, :], squares[:, s:s + 1],
                                            start=(i == 0), stop=(i == GT - 1))
                last.then_inc(var_ready, 1)

            def group_of(k, b, first=False):
                for i in range(GT):
                    if i == SQUARES_AT and not first:
                        sum_squares(k * SLOT_GROUPS + b - 1, (b - 1) % SLOT_GROUPS)
                    sum_tile(b, i, k)

            for b in range(SLOT_GROUPS):
                group_of(0, b, first=(b == 0))
            with pe.Fori(1, ROUNDS) as k:
                for b in range(SLOT_GROUPS):
                    group_of(k, b)
            left = GROUPS - ROUNDS * SLOT_GROUPS
            for b in range(left):
                group_of(ROUNDS, b)
            sum_squares(GROUPS - 1, left - 1)

        @block.scalar
        def _(act):
            act.wait_ge(exp_args_ready, 1)
            nc.scalar.activation(e[:, :, :, :], e[:, :, :, :], ACT.Exp, scale=-2.0).then_inc(exps_ready, 1)
            act.wait_ge(zeros_ready, 1)
            act.wait_ge(table_ready, 1)

            def pivot(turn, b):
                act.wait_ge(pivot_sum_ready, turn + 1)
                nc.scalar.activation(pivot_ps[b][:, :], pivot_ps[b][:, :], ACT.Copy,
                                     scale=-1.0 / (TILE_CH * BANK),
                                     accum_out=neg_pivot[:, b:b + 1]).then_inc(pivot_ready, 1)

            def mean(turn, b):
                act.wait_ge(sums_ready, turn + 1)
                nc.scalar.activation(sum_ps[b][:, :], sum_ps[b][:, :], ACT.Copy, scale=-1.0 / GROUP_N,
                                     accum_out=neg_mean[:, b:b + 1]).then_inc(mean_ready, 1)

            def square(k, b, i, first=False):
                k, b = k + b // SLOT_GROUPS, b % SLOT_GROUPS
                turn, s = k * SLOT_GROUPS + b, b * GT + i
                if i:
                    act.wait_ge(loaded[s], 16 * (k + 1))
                else:
                    act.wait_ge(pivot_ready, turn + 1)
                if not first:
                    act.wait_ge(squares_ready, turn * GT + i)
                nc.scalar.activation(unused[:, :], slot_px(s), ACT.Square, bias=neg_pivot[:, b:b + 1],
                                     accum_out=squares[:, s:s + 1]).then_inc(squares_ready, 1)

            next_fill = act.alloc_register("next_fill")

            def load_fill(turn, i):
                position = (group_at(turn) * GT + i) // TILES_PER_POSITION
                act.reg_load(next_fill, fills[0:1, bass.ds(position, 1)])

            def fill_frame(turn, b, i, first=False):
                tile = turn * GT + i
                entry = act.snap(next_fill, min_val=0,
                                 max_val=(len(SIDES) << EDGE_BITS + ROW_BITS) - 1)
                edge = entry & (1 << EDGE_BITS) - 1
                row = (entry >> EDGE_BITS) & (1 << ROW_BITS) - 1
                side = act.snap(entry >> EDGE_BITS + ROW_BITS)

                def emit(n):
                    rows = SIDES[n]
                    top = row.with_bounds(min_val=0, max_val=H - rows)
                    if not first:
                        act.wait_ge(smooth_ready, tile)
                    nc.scalar.activation(frame_v[:, bass.ds(top + PAD, rows), LEFT:LEFT + W],
                                         xs_v[:, bass.ds(top + (b * GT + i) * H, rows), :],
                                         ACT.Identity, bias=neg_mean[:, b:b + 1]).then_inc(frame_copied, 1)

                choose(act, side, 0, len(SIDES), emit)
                load_fill(*((turn, i + 1) if i + 1 < GT else (turn + 1, 0)))
                act.wait_ge(frame_copied, tile + 1)
                nc.scalar.activation(frame_v[:, PAD:PAD + H, bass.ds(edge.with_bounds(min_val=LEFT - 1, max_val=PITCH - 1), 1)],
                                     zeros[:, :].rearrange("p (r c) -> p r c", c=1),
                                     ACT.Copy).then_inc(frame_ready, 1)

            def deviation(turn):
                act.wait_ge(neg_var_ready, turn + 1)
                nc.scalar.activation(std[:, :], neg_var[:, :], ACT.Sqrt, scale=-1.0).then_inc(std_ready, 1)

            def turn_of(k, b, ahead=GROUPS):
                turn = k * SLOT_GROUPS + b
                act.wait_ge(mean_ready, turn + 1)
                fill_frame(turn, b, 0, first=(ahead == GROUPS - 1))
                if ahead >= 1:
                    square(k, b + 1, 1)
                deviation(turn)
                fill_frame(turn, b, 1)
                if ahead >= 1:
                    square(k, b + 1, 2)
                fill_frame(turn, b, 2)
                if ahead >= 1:
                    mean(turn + 1, (b + 1) % SLOT_GROUPS)
                if ahead >= 2:
                    pivot(turn + 2, (b + 2) % SLOT_GROUPS)
                    square(k, b + 2, 0)

            load_fill(0, 0)
            pivot(0, 0)
            for i in range(GT):
                square(0, 0, i, first=(i == 0))
            mean(0, 0)
            pivot(1, 1)
            square(0, 1, 0)
            for b in range(SLOT_GROUPS):
                turn_of(0, b, ahead=GROUPS - 1 - b)
            with act.Fori(1, ROUNDS) as k:
                for b in range(SLOT_GROUPS):
                    turn_of(k, b)
            left = GROUPS - ROUNDS * SLOT_GROUPS
            for b in range(left):
                turn_of(ROUNDS, b, ahead=left - 1 - b)

        @block.vector
        def _(dve):
            steps = [0]

            def chained(ins):
                steps[0] += 1
                ins.then_inc(setup_step, 1)
                dve.wait_ge(setup_step, steps[0])

            V = nc.vector
            dve.wait_ge(offset_loaded, 16)
            FAR, ROUNDER = 1024.0, 1.5 * 2.0 ** 23
            chained(V.tensor_scalar(off[:, :, :], off[:, :, :], SCALE, FAR, ALU.mult, ALU.min))
            chained(V.tensor_scalar(off[:, :, :], off[:, :, :], -FAR, None, ALU.max))
            chained(V.tensor_scalar(whole[:, :, :], off[:, :, :], ROUNDER, None, ALU.add))
            chained(V.tensor_scalar(whole[:, :, :], whole[:, :, :], ROUNDER, None, ALU.subtract))
            chained(V.tensor_tensor(rest[:, :, :], off[:, :, :], whole[:, :, :], ALU.subtract))
            for k in range(3):
                chained(V.tensor_scalar(tmp[:, :, :], rest[:, :, :], float(k - 1), None, ALU.add))
                last = V.tensor_tensor(e[:, k], tmp[:, :, :], tmp[:, :, :], ALU.mult)
                if k < 2:
                    chained(last)
            last.then_inc(exp_args_ready, 1)

            chained(V.tensor_scalar(whole[:, :, :], whole[:, :, :], float(H), -float(H), ALU.min, ALU.max))
            size_d, below = tmp, norm
            chained(V.scalar_tensor_tensor(size_d[:, :, :], whole[:, :, :], -1.0, whole[:, :, :],
                                           ALU.mult, ALU.max))
            for n, least in enumerate(LEAST[1:]):
                step = float(SIDES[n] - SIDES[n + 1])
                to = kind if n == 0 else below
                chained(V.tensor_scalar(to[:, :, :], size_d[:, :, :], float(least), None, ALU.is_ge))
                if n == 0:
                    chained(V.tensor_scalar(shrink[:, :, :], to[:, :, :], step, None, ALU.mult))
                else:
                    chained(V.tensor_tensor(kind[:, :, :], kind[:, :, :], to[:, :, :], ALU.add))
                    chained(V.scalar_tensor_tensor(shrink[:, :, :], to[:, :, :], step, shrink[:, :, :],
                                                   ALU.mult, ALU.add))
            positive, window, edge, start, first_row = below, size_d, off, rest, shrink
            chained(V.tensor_scalar(positive[:, :, :], whole[:, :, :], 0.0, None, ALU.is_gt))
            chained(V.tensor_tensor(start[:, :, :], shrink[:, :, :], positive[:, :, :], ALU.mult))
            chained(V.tensor_tensor(window[:, :, :], start[:, :, :], whole[:, :, :], ALU.subtract))
            chained(V.scalar_tensor_tensor(edge[:, :, :], positive[:, :, :], float(W + 1), whole[:, :, :],
                                           ALU.mult, ALU.subtract))
            chained(V.tensor_tensor(first_row[:, :, :], shrink[:, :, :], start[:, :, :], ALU.subtract))
            chained(V.tensor_scalar(edge[:, :, 0], edge[:, :, 0], float(LEFT - 1), None, ALU.add))
            chained(V.scalar_tensor_tensor(edge[:, :, 0], first_row[:, :, 1], float(1 << EDGE_BITS), edge[:, :, 0],
                                           ALU.mult, ALU.add))
            chained(V.scalar_tensor_tensor(fills[:, :], kind[:, :, 1], float(1 << EDGE_BITS + ROW_BITS),
                                           edge[:, :, 0], ALU.mult, ALU.add))
            chained(V.scalar_tensor_tensor(parts[:, KIND], kind[:, :, 1], float(len(SIDES)),
                                           kind[:, :, 0], ALU.mult, ALU.add))
            chained(V.scalar_tensor_tensor(parts[:, TO], start[:, :, 1], float(W), start[:, :, 0],
                                           ALU.mult, ALU.add))
            chained(V.scalar_tensor_tensor(edge[:, :, 1], window[:, :, 1], float(PITCH), window[:, :, 0],
                                           ALU.mult, ALU.add))
            chained(V.tensor_scalar(parts[:, FROM], edge[:, :, 1], float(PAD * PITCH + LEFT), None, ALU.add))
            chained(V.tensor_scalar(parts[:, TO], parts[:, TO], KIND_BITS, None, ALU.logical_shift_left))
            chained(V.tensor_scalar(parts[:, FROM], parts[:, FROM], KIND_BITS + TO_BITS, None,
                                    ALU.logical_shift_left))
            chained(V.tensor_tensor(windows[:, :], parts[:, KIND], parts[:, TO], ALU.bitwise_or))
            V.tensor_tensor(windows[:, :], windows[:, :], parts[:, FROM], ALU.bitwise_or).then_inc(table_ready, 1)

            dve.wait_ge(exps_ready, 1)
            chained(V.tensor_tensor(norm[:, :, :], e[:, 0], e[:, 1], ALU.add))
            chained(V.tensor_tensor(norm[:, :, :], norm[:, :, :], e[:, 2], ALU.add))
            chained(V.reciprocal(norm[:, :, :], norm[:, :, :]))
            chained(V.reciprocal(tmp[:, :, 0], e[:, 1, :, 0]))
            chained(V.tensor_tensor(side_w[:, :, 0], e[:, 0, :, 0], tmp[:, :, 0], ALU.mult))
            chained(V.tensor_tensor(side_w[:, :, 1], e[:, 2, :, 0], tmp[:, :, 0], ALU.mult))
            chained(V.tensor_tensor(tmp[:, :, 0], e[:, 1, :, 0], norm[:, :, 0], ALU.mult))
            chained(V.tensor_tensor(tmp[:, :, 0], tmp[:, :, 0], norm[:, :, 1], ALU.mult))
            for k in range(3):
                last = V.tensor_tensor(base_w[:, :, k], e[:, k, :, 1], tmp[:, :, 0], ALU.mult)
            last.then_inc(tile_done, 1)

            STD_STEPS = 6

            def variance(turn, b):
                dve.wait_ge(var_ready, turn + 1)
                V.tensor_scalar(square_mean[:, :], var_ps[:, 0:1], 1.0 / GROUP_N, EPS, ALU.mult,
                                ALU.add).then_inc(std_step, 1)
                dve.wait_ge(mean_ready, turn + 1)
                V.tensor_tensor(mean_off[:, :], neg_pivot[:, bass.ds(b, 1)], neg_mean[:, bass.ds(b, 1)],
                                ALU.subtract).then_inc(std_step, 1)
                dve.wait_ge(std_step, STD_STEPS * turn + 2)
                V.scalar_tensor_tensor(neg_var[:, :], mean_off[:, :], mean_off[:, :], square_mean[:, :],
                                       ALU.mult, ALU.subtract).then_inc(neg_var_ready, 1)

            def reciprocal_std(turn):
                dve.wait_ge(std_ready, turn + 1)
                V.reciprocal(rstd0[:, :], std[:, :]).then_inc(std_step, 1)
                dve.wait_ge(std_step, STD_STEPS * turn + 3)
                V.tensor_scalar(fix[:, 0:1], neg_var[:, :], rstd0[:, :], rstd0[:, :], ALU.mult,
                                ALU.mult).then_inc(std_step, 1)
                dve.wait_ge(std_step, STD_STEPS * turn + 4)
                V.tensor_scalar(fix[:, 1:2], fix[:, 0:1], 0.5, 1.5, ALU.mult, ALU.add).then_inc(std_step, 1)
                dve.wait_ge(std_step, STD_STEPS * turn + 5)
                V.tensor_tensor(rstd[:, :], fix[:, 1:2], rstd0[:, :], ALU.mult).then_inc(std_step, 1)
                dve.wait_ge(std_step, STD_STEPS * turn + 6)

            def smooth_tile(rows, cols, turn, i, done, position, follows, src, dst):
                around = frame[:, bass.ds(src - 1, rows * PITCH + 2)]
                under = xs[:, bass.ds(dst, rows * W)]

                def frame_window(shift):
                    v = around[:, 1 + shift:1 + shift + rows * PITCH]
                    return v.rearrange("p (r c) -> p r c", c=PITCH)[:, :, 0:cols]

                def x_window(a, b):
                    return under.rearrange("p (r c) -> p r c", c=W)[:, a:b, 0:cols]

                def column_weights():
                    V.tensor_scalar(col_w[:, :], base_w[:, bass.ds(position, 1), :].rearrange("p a k -> p (a k)"),
                                    rstd[:, :], None, ALU.mult).then_inc(col_w_ready, 1)

                dve.wait_ge(tile_done, done)
                sm = smooth[:, 0:rows * cols].rearrange("p (r c) -> p r c", c=cols)
                V.scalar_tensor_tensor(sm, frame_window(-1), side_w[:, bass.ds(position, 1), 0], frame_window(0),
                                       ALU.mult, ALU.add
                                       ).wait_op(frame_ready, done_count, "sem-ge").then_inc(half_smooth, 1)
                load_window(follows)
                if i > 0:
                    column_weights()
                V.scalar_tensor_tensor(sm, frame_window(1), side_w[:, bass.ds(position, 1), 1], sm,
                                       ALU.mult, ALU.add
                                       ).wait_op(half_smooth, done_count, "sem-ge").then_inc(smooth_ready, 1)
                if i == 0:
                    reciprocal_std(turn)
                    column_weights()
                dve.wait_ge(col_w_ready, done)
                V.scalar_tensor_tensor(x_window(0, rows), sm, col_w[:, 1:2], x_window(0, rows),
                                       ALU.mult, ALU.add
                                       ).wait_op(smooth_ready, done_count, "sem-ge").then_inc(centre_added, 1)
                V.scalar_tensor_tensor(x_window(1, rows), sm[:, 0:rows - 1], col_w[:, 0:1], x_window(1, rows),
                                       ALU.mult, ALU.add
                                       ).wait_op(centre_added, done_count, "sem-ge").then_inc(above_added, 1)
                V.scalar_tensor_tensor(x_window(0, rows - 1), sm[:, 1:rows], col_w[:, 2:3], x_window(0, rows - 1),
                                       ALU.mult, ALU.add
                                       ).wait_op(above_added, done_count, "sem-ge").then_inc(tile_done, 1)

            to_pixel = dve.alloc_register("to_pixel")
            from_pixel = dve.alloc_register("from_pixel")
            done_count = dve.alloc_register("done_count")
            this_source = dve.alloc_register("this_source")
            next_source = dve.alloc_register("next_source")

            def keep(register, value, most):
                dve.reg_mov(register, value)
                return dve.snap(register, min_val=0, max_val=most)

            next_window = dve.alloc_register("next_window")

            def load_window(position):
                dve.reg_load(next_window, windows[0:1, bass.ds(position, 1)])

            TO_NEXT = STRIDE * GT - (GT - 1)

            def tile_of(turn, base, i):
                done = keep(done_count, dve.snap(done_count, min_val=0, max_val=TILES - 1) + 1, TILES)
                source = keep(this_source, next_source, TILES - 1)
                position = source // TILES_PER_POSITION
                follows = keep(next_source, source + 1 if i + 1 < GT else (source + TO_NEXT) % TILES,
                               TILES - 1) // TILES_PER_POSITION
                entry = dve.snap(next_window, min_val=0, max_val=(FRAME_ROWS * PITCH << KIND_BITS + TO_BITS) - 1)
                kind_of = dve.snap(entry & (1 << KIND_BITS) - 1)
                dst = keep(to_pixel, base + i * PIX + ((entry >> KIND_BITS) & (1 << TO_BITS) - 1), SLOTS * PIX)
                src = keep(from_pixel, entry >> KIND_BITS + TO_BITS, FRAME_ROWS * PITCH)

                def emit(code):
                    ky, kx = divmod(code, len(SIDES))
                    rows, cols = SIDES[ky], SIDES[kx]
                    most = (PAD + MOST[ky]) * PITCH + LEFT + MOST[kx]
                    smooth_tile(rows, cols, turn, i, done, position, follows,
                                src.with_bounds(min_val=1, max_val=most),
                                dst.with_bounds(min_val=0, max_val=(SLOTS - 1) * PIX + (H - rows) * W + W - cols))

                choose(dve, kind_of, 0, len(SIDES) ** 2, emit)

            dve.wait_ge(table_ready, 1)
            dve.reg_mov(done_count, 0)
            dve.reg_mov(next_source, group_at(0) * GT)
            load_window(group_at(0) * GT // TILES_PER_POSITION)
            with dve.Fori(0, GROUPS) as turn:
                variance(turn, turn % SLOT_GROUPS)
                base = (turn % SLOT_GROUPS) * (GT * PIX)
                for i in range(GT):
                    tile_of(turn, base, i)


def kernel(x, L0_conv_offset):
    import numpy as np
    import concourse.bacc as bacc
    from concourse.bass_utils import run_bass_kernel_spmd

    nc = bacc.Bacc("TRN2", target_bir_lowering=False, num_devices=1)
    arrays = {"x_dram": np.ascontiguousarray(x), "offset_dram": np.ascontiguousarray(L0_conv_offset)}
    aps = [nc.dram_tensor(name, a.shape, mybir.dt.from_np(a.dtype), kind="ExternalInput").ap()
           for name, a in arrays.items()]
    out = nc.dram_tensor("out_dram", x.shape, mybir.dt.float32, kind="ExternalOutput").ap()
    build(nc, *aps, out)
    r = run_bass_kernel_spmd(nc, [arrays], core_ids=[0])
    return r.results[0]["out_dram"]
```
